# Optimizing a Trainium2 kernel written in Bass

```python
import numpy as np
import jax
import jax.numpy as jnp

def _softmax(x, axis=-1):
    return jax.nn.softmax(x, axis=axis)

def _gelu(x):
    return jax.nn.gelu(x, approximate=True)

def _silu(x):
    return jax.nn.silu(x)

def _sigmoid(x):
    return jax.nn.sigmoid(x)

def _layernorm(x, axis=-1, eps=1e-05):
    m = jnp.mean(x, axis=axis, keepdims=True)
    v = jnp.var(x, axis=axis, keepdims=True)
    return (x - m) / jnp.sqrt(v + eps)

def _scatter_add(tgt, idx, src, axis=0):
    return tgt.at[idx].add(src)

def _segment_sum(src, seg, n):
    return jax.ops.segment_sum(src, seg, n)
kernel_name = 'mk_gnn_ffn_d1_gnn_r8_84f354'

def setup_inputs(seed: int=0):
    np.random.seed(seed)
    _w = jnp.asarray

    def _rec_inputs():
        import jax
        import jax.numpy as jnp
        _gk = jax.random.key(seed)
        x = -0.0002117 + 1 * jax.random.normal(jax.random.fold_in(_gk, 1), (6250, 256), jnp.float32)
        _s = jax.random.randint(jax.random.fold_in(_gk, 2), (100000,), 0, 6250, jnp.int32)
        _d = jax.random.randint(jax.random.fold_in(_gk, 3), (100000,), 0, 6250, jnp.int32)
        _loop = jnp.arange(6250, dtype=jnp.int32)
        src = jnp.concatenate([_s, _d, _loop])
        dst = jnp.concatenate([_d, _s, _loop])
        _o = jnp.argsort(dst, stable=True)
        src = src[_o]
        dst = dst[_o]
        return (x, src, dst)
    x, src, dst = _rec_inputs()

    def _L0_gnn_setup():
        import jax, jax.numpy as jnp
        import numpy as np
        N_NODES = 12500
        N_EDGES = 40000
        D_IN, D_HID, D_OUT = (256, 1024, 256)
        BN_EPS = 1e-05
        key = jax.random.key(seed)
        ks = jax.random.split(key, 6)
        x = jax.random.normal(ks[0], (N_NODES, D_IN), dtype=jnp.float32)
        edge_index = jax.random.randint(ks[1], (2, N_EDGES), 0, N_NODES, dtype=jnp.int64)
        W1 = jax.random.normal(ks[2], (D_IN, D_HID), dtype=jnp.float32) * (1.0 / np.sqrt(D_IN))
        b1 = jnp.zeros((D_HID,), dtype=jnp.float32)
        gamma = jnp.ones((D_HID,), dtype=jnp.float32)
        beta = jnp.zeros((D_HID,), dtype=jnp.float32)
        W2 = jax.random.normal(ks[3], (D_HID, D_OUT), dtype=jnp.float32) * (1.0 / np.sqrt(D_HID))
        b2 = jnp.zeros((D_OUT,), dtype=jnp.float32)
        return {'x': x, 'edge_index': edge_index, 'W1': W1, 'b1': b1, 'gamma': gamma, 'beta': beta, 'W2': W2, 'b2': b2}
    _L0_gnn_all = _L0_gnn_setup()
    _L0_gnn_in = {k: v for k, v in _L0_gnn_all.items() if k in ('W1', 'b1', 'gamma', 'beta', 'W2', 'b2')}
    del _L0_gnn_all

    def _L0_ffn_setup():
        import jax, jax.numpy as jnp
        import numpy as np
        NUM_EXPERTS = 8
        TOP_K = 2
        B, S, D = (8, 1024, 256)

        def _moe(tokens, router_w, w1, b1, w2, b2):
            N = tokens.shape[0]
            E = router_w.shape[0]
            logits = tokens.astype(jnp.float32) @ router_w.astype(jnp.float32).T
            probs = jax.nn.softmax(logits, axis=-1)
            rw, re = jax.lax.top_k(probs, TOP_K)
            if TOP_K > 1:
                rw = rw / jnp.maximum(rw.sum(-1, keepdims=True), 1e-12)
            rw = rw.astype(tokens.dtype)
            combine = jnp.zeros((N, E), tokens.dtype).at[jnp.arange(N)[:, None], re].set(rw)
            out = tokens
            for e in range(E):
                h = jax.nn.gelu(tokens @ w1[e] + b1[e], approximate=False)
                y = h @ w2[e] + b2[e]
                out = out + combine[:, e:e + 1] * y
            return out
        key = jax.random.key(seed)
        ks = jax.random.split(key, 4)
        scale = 1.0 / np.sqrt(D).astype(np.float32)
        return {'input_embeddings': jax.random.normal(ks[0], (B, S, D), jnp.float32), 'router_w': jax.random.normal(ks[1], (NUM_EXPERTS, D), jnp.float32) * scale, 'w1': jax.random.normal(ks[2], (NUM_EXPERTS, D, D), jnp.float32) * scale, 'b1': jnp.zeros((NUM_EXPERTS, D), jnp.float32), 'w2': jax.random.normal(ks[3], (NUM_EXPERTS, D, D), jnp.float32) * scale, 'b2': jnp.zeros((NUM_EXPERTS, D), jnp.float32)}
    _L0_ffn_all = _L0_ffn_setup()
    _L0_ffn_in = {k: v for k, v in _L0_ffn_all.items() if k in ('router_w', 'w1', 'b1', 'w2', 'b2')}
    del _L0_ffn_all
    return {'x': x, 'src': src, 'dst': dst, 'L0_gnn_W1': _L0_gnn_in['W1'], 'L0_gnn_b1': _L0_gnn_in['b1'], 'L0_gnn_gamma': _L0_gnn_in['gamma'], 'L0_gnn_beta': _L0_gnn_in['beta'], 'L0_gnn_W2': _L0_gnn_in['W2'], 'L0_gnn_b2': _L0_gnn_in['b2'], 'L0_ffn_router_w': _L0_ffn_in['router_w'], 'L0_ffn_w1': _L0_ffn_in['w1'], 'L0_ffn_b1': _L0_ffn_in['b1'], 'L0_ffn_w2': _L0_ffn_in['w2'], 'L0_ffn_b2': _L0_ffn_in['b2']}

def reference(x, src, dst, L0_gnn_W1, L0_gnn_b1, L0_gnn_gamma, L0_gnn_beta, L0_gnn_W2, L0_gnn_b2, L0_ffn_router_w, L0_ffn_w1, L0_ffn_b1, L0_ffn_w2, L0_ffn_b2):
    import jax
    import jax.numpy as jnp

    def _L0_gnn_ref(x, edge_index, W1, b1, gamma, beta, W2, b2):
        import jax, jax.numpy as jnp
        import numpy as np
        N_NODES = 12500
        N_EDGES = 40000
        D_IN, D_HID, D_OUT = (256, 1024, 256)
        BN_EPS = 1e-05
        src, dst = (edge_index[0], edge_index[1])
        agg = jax.ops.segment_sum(x[src], dst, num_segments=x.shape[0])
        h = agg + x
        h1 = h @ W1 + b1
        mean = jnp.mean(h1, axis=0)
        var = jnp.mean(jnp.square(h1 - mean), axis=0)
        h1 = (h1 - mean) * jax.lax.rsqrt(var + BN_EPS) * gamma + beta
        h1 = jax.nn.relu(h1)
        out = jax.nn.relu(h1 @ W2 + b2)
        return out

    def _L0_ffn_ref(input_embeddings, router_w, w1, b1, w2, b2):
        import jax, jax.numpy as jnp
        import numpy as np
        NUM_EXPERTS = 8
        TOP_K = 2
        B, S, D = (8, 1024, 256)

        def _moe(tokens, router_w, w1, b1, w2, b2):
            N = tokens.shape[0]
            E = router_w.shape[0]
            logits = tokens.astype(jnp.float32) @ router_w.astype(jnp.float32).T
            probs = jax.nn.softmax(logits, axis=-1)
            rw, re = jax.lax.top_k(probs, TOP_K)
            if TOP_K > 1:
                rw = rw / jnp.maximum(rw.sum(-1, keepdims=True), 1e-12)
            rw = rw.astype(tokens.dtype)
            combine = jnp.zeros((N, E), tokens.dtype).at[jnp.arange(N)[:, None], re].set(rw)
            out = tokens
            for e in range(E):
                h = jax.nn.gelu(tokens @ w1[e] + b1[e], approximate=False)
                y = h @ w2[e] + b2[e]
                out = out + combine[:, e:e + 1] * y
            return out
        b, s, d = input_embeddings.shape
        tokens = input_embeddings.reshape(b * s, d)
        return _moe(tokens, router_w, w1, b1, w2, b2).reshape(b, s, d)
    edge_index = jnp.stack([src, dst])
    x = x + _L0_gnn_ref(_layernorm(x, axis=-1), edge_index, L0_gnn_W1, L0_gnn_b1, L0_gnn_gamma, L0_gnn_beta, L0_gnn_W2, L0_gnn_b2)
    x = x + _L0_ffn_ref(_layernorm(x, axis=-1)[None], L0_ffn_router_w, L0_ffn_w1, L0_ffn_b1, L0_ffn_w2, L0_ffn_b2)[0]
    return x

_drawn_inputs = setup_inputs


def setup_inputs(seed=0):
    import zlib

    import numpy as np

    out = dict(_drawn_inputs(seed))
    spreads = {'L0_gnn_b1': (0.0, 0.8),
     'L0_gnn_gamma': (1.0, 0.2),
     'L0_gnn_beta': (0.0, 0.1),
     'L0_gnn_b2': (0.0, 0.1),
     'L0_ffn_b1': (0.0, 0.346),
     'L0_ffn_b2': (0.0, 0.1)}
    factors = {}
    for name, (base, spread) in spreads.items():
        noise = np.random.default_rng([zlib.crc32(name.encode()), seed]).standard_normal(out[name].shape)
        drawn = base * np.exp(spread * noise) if base else spread * noise
        out[name] = jnp.asarray(drawn.astype(out[name].dtype))
    for name, factor in factors.items():
        out[name] = (out[name] * factor).astype(out[name].dtype)
    return out
```

```python
from contextlib import ExitStack

import concourse.bass as bass
from concourse import mybir

F32 = mybir.dt.float32
F32R = mybir.dt.float32r
I32 = mybir.dt.int32
F16 = mybir.dt.float16
ALU = mybir.AluOpType
ACT = mybir.ActivationFunctionType
AX = mybir.AxisListType

LN_EPS = 1e-5
X_SCALE = 256.0
BN_EPS = 1e-5


PRIMED = dict(counted=5, oh=1, adj=3, xn_stored=1, h_T=1, h_split=1, h1_copied=4, h1_stat=16, h1st_free=2, mm_w1=9, relu_step=2, mm_w2=8, r_lo=8, psO_read=3, tok_T=1, tTs=1, router=1, tT_stored=1, logits=1, scattered=1, t_split=3, mm1=17, comb_T=1, b2mm=1, g_split=3, mm2=2, y_added=3, gelu=3, acc=1)


class Event:

    def __init__(self, sem, primed):
        self.sem, self.primed = sem, primed

    def wait(self, eng, count):
        eng.wait_ge(self.sem, count + self.primed)

    def wait_alone(self, eng, count, tally):
        eng.wait_ge(self.sem, count + self.primed)
        eng.sem_inc(tally.sem, 1)


def gnn_moe(nc, x, src, dst, W1, b1, gamma, beta, W2, b2, router_w, ew1, eb1, ew2, eb2, out):
    N, D = x.shape
    E = src.shape[0]
    HID = W1.shape[1]
    NX = ew1.shape[0]
    P = 125
    NT = N // P
    A = 2
    S = NT // A
    C = A * P
    KD = D // 128
    KH = HID // 128
    EC = E // P
    G = 5
    NG = N // G
    SG = C // G
    GW = G * NT
    JB = SG // 2
    CH = 128
    Q = 32
    NR = E // Q + CH // Q + 1
    NP = (NR - 1) * Q + CH - E
    BL = 330
    NB = E // BL
    XG, XT = 5, NT // 5
    TG = NG // P
    RING = 5
    assert NT * P == N and S * A == NT and EC * P == E and KD * 128 == D and KH * 128 == HID
    assert NB * BL == E and TG * P == NG and JB * 2 == SG and JB % RING == 0 and TG % 2 == 0

    xn_d = nc.dram_tensor("xn_rows", (N, D), F32, kind="Internal").ap()
    agg_d = nc.dram_tensor("agg_rows", (N, D), F32, kind="Internal").ap()
    word_d = nc.dram_tensor("edge_words", (E + NP,), I32, kind="Internal").ap()
    chunk_d = nc.dram_tensor("edge_chunks", (NR, CH), I32, kind="Internal").ap()
    tT_d = nc.dram_tensor("tok_cols", (S, 128, KD * C), F32, kind="Internal").ap()
    h1_d = nc.dram_tensor("h1_cols", (S, 128, KH * C), F32, kind="Internal").ap()

    with ExitStack() as ctx:
        def sb(name, shape, dt=F32):
            return ctx.enter_context(nc.sbuf_tensor(name, shape, dt))

        events = {}

        def ev(name, primed=0):
            if name not in events:
                events[name] = Event(ctx.enter_context(nc.semaphore("s_" + name)), primed)
            return events[name]

        for n, count in PRIMED.items():
            ev(n, count)

        ident = sb("ident", [128, 128])
        w2hi, w2lo = sb("w2hi", [128, KH, D], F32R), sb("w2lo", [128, KH, D], F32R)
        b2bc = sb("b2bc", [P, 1, D])
        rw_rows, rwT = sb("rw_rows", [NX, D]), sb("rwT", [128, KD, NX])
        eb1T = sb("eb1T", [128, NX, KD])
        eb2x = sb("eb2x", [A * NX, A * D])
        bnp = sb("bnp", [128, 3, KH])
        bns = sb("bns", [128, 8, KH])
        hmv = sb("hmv", [128, KH, 2])
        L = sb("L", [P, NT, NX])
        gm = sb("gm", [P, 4, NT])
        mv = sb("mv", [P, NT, 2])
        rs = sb("rs", [P, 5, NT])
        flag_f, flag = sb("flag_f", [1, 1]), sb("flag", [1, 1], I32)

        def over(*plan):
            with ExitStack() as room:
                return [room.enter_context(nc.sbuf_tensor(n, s, d)) for n, s, d in plan]

        xhi, xlo = over(("xhi", [P, NT, D], F16), ("xlo", [P, NT, D], F16))
        e1hi, e1lo, estage = over(("e1hi", [128, NX, KD, D], F32R), ("e1lo", [128, NX, KD, D], F32R),
                                  ("estage", [128, NX, KD, D], F32))
        sb("region_x", [P, NT, D])
        adj, = over(("adj", [P, 2, NT, C], F16))
        xs = sb("xs", [P, NT, D])
        y1 = [("w1hi", [128, KD, HID], F32R), ("w1lo", [128, KD, HID], F32R), ("h1st", [128, 2, KH * 256], F32),
              ("keyT", [CH, 2 * NG], F16), ("slT", [CH, 2 * NG], F16), ("iota16", [CH, GW], F16), ("iota_i", [CH, GW], I32),
              ("ones", [P, P], F32), ("ident16", [P, P], F16), ("st6", [P, NT, 6], F32)]
        y1 += [("starts", [P, 4, TG], F32), ("idx_b", [P, TG], I32), ("idx_c", [P, 2, TG], I32), ("base_g", [P, TG], F32),
               ("thr", [P, TG], F32), ("thr_i", [P, TG], I32), ("base_i", [P, TG], I32), ("hits", [P, 2], F32)]
        named = lambda tag, plan: [(tag + n, s, d) for n, s, d in plan]
        (w1hi, w1lo, h1st, keyT, slT, iota16, iota_i, ones, ident16, st6, starts, idx_b, idx_c, base_g, thr, thr_i, base_i, hits,
         hhi, hlo, hstat, oh_s, oh_k, steps_k, xst) = over(
            *y1, ("hhi", [128, 2, KD, C], F32R), ("hlo", [128, 2, KD, C], F32R), ("hstat", [128, KH, S, 6], F32),
            ("oh_s", [CH, RING, 4, CH], F16), ("oh_k", [CH, RING, 4, GW], F16), ("steps_k", [CH, 2, 2 * SG], F32),
            ("xst", [P, 2, A, D], F16))
        (*_, src_i, dst_i, sh_i, word_i, idx_first, fblk, pad_w) = over(
            *named("a_", y1), ("src_i", [P, EC], I32), ("dst_i", [P, EC], I32), ("sh_i", [P, EC], I32), ("word_i", [P, EC], I32),
            ("idx_first", [1, NB], I32), ("fblk", [1, NB], F32), ("pad_w", [1, NP], I32))
        TH = TG // 2
        (*_, chunks, c_key, c_sl, c_tmp) = over(
            *named("b_", y1), ("chunks", [P, TG, 2, CH], I32), ("c_key", [P, TH, 2 * CH], F32),
            ("c_sl", [P, TH, 2 * CH], F32), ("c_tmp", [P, TH, 2 * CH], I32))
        (*_, blk) = over(*named("c_", y1[:2]), ("blk", [P, TG, BL], I32))
        (*_, _, _, _, hb, isrc, idst, iput, fdst, rank, fput, diag, sel, selb, grow, cur, newr, src_t, dst_t, ones_g, before_g) = over(
            *named("d_", y1), ("d_hhi", [128, 2, KD, C], F32R), ("d_hlo", [128, 2, KD, C], F32R), ("d_hstat", [128, KH, S, 6], F32),
            ("hb", [P, A, D], F32), ("isrc", [P, 1], I32), ("idst", [P, 1], I32), ("iput", [P, 1], I32),
            ("fdst", [P, 1], F32), ("rank", [P, 1], F32), ("fput", [P, 1], F32),
            ("diag", [P, P], F32), ("sel", [P, P], F32), ("selb", [P, P], F32),
            ("grow", [P, D], F32), ("cur", [P, D], F32), ("newr", [P, D], F32),
            ("src_t", [P, EC], I32), ("dst_t", [P, EC], I32), ("ones_g", [P, P], F32), ("before_g", [P, P], F32))
        stage = h1st[:, 0, :]
        y = [("e2hi", [128, NX, KD, D], F32R), ("e2lo", [128, NX, KD, D], F32R)]
        (e2hi, e2lo, hin, rf, rhi, rlo, vt, tok, tTs, s6b, mvb, rsb) = over(
            *y, ("hin", [128, 2, KH * C], F32), ("rf", [128, KH, C], F32),
            ("rhi", [128, KH, C], F32R), ("rlo", [128, KH, C], F32R), ("vt", [P, A, D], F32),
            ("tok", [P, A, D], F32), ("tTs", [128, KD, C], F32), ("s6b", [P, A, 6], F32),
            ("mvb", [P, A, 2], F32), ("rsb", [P, 6, A], F32))
        gk_gt = [("gk", [P, NT, NX], F32), ("gt", [P, NT, NX], F32)]
        (_, _, gk, gt, tin, thi, tlo, gf, ghi, glo, cst, cT) = over(
            ("y_e2hi", [128, NX, KD, D], F32R), ("y_e2lo", [128, NX, KD, D], F32R), *gk_gt,
            ("tin", [128, 2, KD * C], F32), ("thi", [128, 2, KD, C], F32R), ("tlo", [128, 2, KD, C], F32R),
            ("gf", [128, 2, KD, C], F32), ("ghi", [128, 2, KD, C], F32R), ("glo", [128, 2, KD, C], F32R),
            ("cst", [P, A * NX], F32), ("cT", [A * NX, P], F32))

        ps = ctx.enter_context(nc.psum_tensor("ps", [128, 8, 512], F32))
        x_t, xn_t, agg_t, out_t = (v.rearrange("(t p) d -> p t d", p=P) for v in (x, xn_d, agg_d, out))
        block = ctx.enter_context(nc.Block())

        def quick(eng):
            ev("flag").wait(eng, 1)
            return eng.If(eng.value_load(flag[0:1, 0:1], min_val=0, max_val=1) == 1)

        def order(first, last):
            work = [("B", 0), ("B", 1), ("B", 2), ("F", 0), ("F", 1)]
            f = 2
            for j in range(JB):
                work.append(("G", j))
                if j + 3 < JB:
                    work.append(("B", j + 3))
                if j % 2 == 1 and f < KH:
                    work += [("F", f), ("F", f + 1)][:1]
                    f += 1
            return [w for w in work if not (first and w[0] == "F") and not (last and w[0] == "B")]

        @block.sync
        def _(sp):
            for e in events.values():
                if e.primed:
                    sp.sem_inc(e.sem, e.primed)
            sp.dma_start(src_i[:, :], src.rearrange("(p c) -> p c", p=P)).then_inc(ev("ld_src").sem, 16)
            sp.dma_start(dst_i[:, :], dst.rearrange("(p c) -> p c", p=P)).then_inc(ev("ld_dst").sem, 16)
            with nc.allow_non_contiguous_dma(reason="every block's first destination"):
                sp.dma_start(idx_first[:, :], dst.rearrange("(c b) -> b c", b=BL)[0:1, :]).then_inc(ev("ld_first").sem, 16)
            sp.dma_start(xs[:, :, :], x_t).then_inc(ev("ld_x").sem, 16)
            sp.dma_start(rw_rows[:, :], router_w).then_inc(ev("ld_rw").sem, 16)
            with nc.allow_non_contiguous_dma(reason="small parameter vectors by partition"):
                for j, v in enumerate((b1, gamma, beta)):
                    sp.dma_start(bnp[:, j, :], v.rearrange("(m p) -> p m", p=128)).then_inc(ev("ld_bn").sem, 16)
                for k in range(KD):
                    sp.dma_start(eb1T[:, :, k], eb1.rearrange("e (k p) -> p e k", p=128)[:, :, k]).then_inc(ev("ld_eb1").sem, 16)
            sp.dma_start(b2bc[:, 0, :], b2.rearrange("(a d) -> a d", a=1).broadcast_to([P, D])).then_inc(ev("ld_b2").sem, 16)
            ev("zeroed").wait(sp, 1)
            for a in range(A):
                sp.dma_start(eb2x[a * NX:(a + 1) * NX, a * D:(a + 1) * D], eb2).then_inc(ev("ld_eb2").sem, 16)
            ev("pad").wait(sp, 1)
            sp.dma_start(word_d[E:E + NP].rearrange("(a n) -> a n", a=1), pad_w[:, :]).then_inc(ev("st_words").sem, 16)
            ev("words").wait(sp, 1)
            sp.dma_start(word_d[0:E].rearrange("(p c) -> p c", p=P), word_i[:, :]).then_inc(ev("st_words").sem, 16)
            ev("st_words").wait(sp, 32)
            every_q = bass.AP(tensor=word_d.tensor, offset=0, ap=[[Q, NR], [1, CH]])
            sp.dma_start(chunk_d, every_q).then_inc(ev("st_chunks").sem, 16)
            ev("starts").wait(sp, 1)
            sp.dma_start(stage.rearrange("p (k h) -> p k h", k=KD), W1.rearrange("(k p) h -> p k h", p=128)).then_inc(ev("ld_w1").sem, 16)
            ev("w_split").wait(sp, 2)
            sp.dma_start(stage.rearrange("p (k h) -> p k h", k=KH), W2.rearrange("(k p) h -> p k h", p=128)).then_inc(ev("ld_w2").sem, 16)
            def load_h(i):
                ev("h_T").wait(sp, i)
                sp.dma_start(hb[:, :, :], agg_t[:, bass.ds(i * A, A), :]).then_inc(ev("ld_h").sem, 16)

            def store_h1(i):
                ev("h1_copied").wait(sp, (i + 1) * (KH // 2))
                sp.dma_start(h1_d[bass.ds(i, 1), :, :].rearrange("a p (k n) -> p (a k) n", n=C),
                             h1st[:, bass.ds(i % 2, 1), :].rearrange("p a (k n) -> p (a k) n", n=256)[:, :, 0:C]
                             ).then_inc(ev("st_h1").sem, 16)

            with quick(sp):
                with sp.Fori(0, S) as i:
                    store_h1(i)
                    ev("st_h1").wait(sp, i * 16 + 16)
                    sp.sem_inc(ev("h1st_free").sem, 1)
            with sp.Else():
                sp.dma_start(src_t[:, :], src.rearrange("(p c) -> p c", p=P)).then_inc(ev("ld_src").sem, 16)
                sp.dma_start(dst_t[:, :], dst.rearrange("(p c) -> p c", p=P)).then_inc(ev("ld_dst").sem, 16)
                with sp.Fori(0, NT) as t:
                    ev("xn_row").wait(sp, t + 1)
                    sp.dma_start(xn_t[:, bass.ds(t, 1), :].rearrange("p a n -> p (a n)"), newr[:, :]).then_inc(ev("st_xn").sem, 16)
                    sp.dma_start(agg_t[:, bass.ds(t, 1), :].rearrange("p a n -> p (a n)"), newr[:, :]).then_inc(ev("st_agg").sem, 16)
                    ev("st_xn").wait(sp, t * 16 + 16)
                    ev("st_agg").wait(sp, t * 16 + 16)
                    sp.sem_inc(ev("xn_stored").sem, 1)
                ev("edges_done").wait(sp, 1)
                load_h(0)
                with sp.Fori(0, S - 1) as i:
                    load_h(i + 1)
                    store_h1(i)
                    ev("st_h1").wait(sp, i * 16 + 16)
                    sp.sem_inc(ev("h1st_free").sem, 1)
                store_h1(S - 1)
            ev("st_h1").wait(sp, S * 16)
            ev("bn_done").wait(sp, 1)
            sp.dma_start(xs[:, :, :], x_t).then_inc(ev("ld_x").sem, 16)
            sp.dma_start(estage[:, :, :, :], ew1.rearrange("e (k p) h -> p e k h", p=128)).then_inc(ev("ld_e1").sem, 16)

            with sp.Fori(0, S) as i:
                ev("relu_step").wait(sp, i - 1)
                sp.dma_start(hin[:, bass.ds(i % 2, 1), :].rearrange("p a n -> p (a n)"),
                             h1_d[bass.ds(i, 1), :, :].rearrange("a p n -> p (a n)")).then_inc(ev("ld_h1").sem, 16)
                ev("ld_h1").wait(sp, i * 16 + 16)
                sp.sem_inc(ev("hin_ready").sem, 1)
            ev("e1_split").wait(sp, 2)
            sp.dma_start(estage[:, :, :, :], ew2.rearrange("e (k p) h -> p e k h", p=128)).then_inc(ev("ld_e2").sem, 16)
            ev("tT_stored").wait(sp, S)
            ev("gnn_done").wait(sp, 1)

            def load_t(i):
                ev("t_split").wait(sp, 2 * (i - 1))
                sp.dma_start(tin[:, bass.ds(i % 2, 1), :].rearrange("p a n -> p (a n)"),
                             tT_d[bass.ds(i, 1), :, :].rearrange("a p n -> p (a n)")).then_inc(ev("ld_t").sem, 16)
                ev("ld_t").wait(sp, i * 16 + 16)
                sp.sem_inc(ev("tin_ready").sem, 1)

            def store_out(i):
                ev("acc").wait(sp, i + 1)
                sp.dma_start(out_t[:, bass.ds(i * A, A), :], xs[:, bass.ds(i * A, A), :]).then_inc(ev("st_out").sem, 16)

            load_t(0)
            with sp.Fori(0, S - 1) as i:
                load_t(i + 1)
                store_out(i)
            store_out(S - 1)
            ev("st_out").wait(sp, S * 16)

        def sum_over_edges(gp):
            with gp.Fori(0, EC) as c:
                ev("index").wait_alone(gp, c * 2 + 2, ev("pool_tally"))
                gp.indirect_dma_start(grow[:, :], None, xn_d, bass.IndirectOffsetOnAxis(ap=isrc[:, 0:1], axis=0)
                                      ).then_inc(ev("gathered").sem, 16)
                ev("scattered").wait_alone(gp, c, ev("pool_tally"))
                gp.indirect_dma_start(cur[:, :], None, agg_d, bass.IndirectOffsetOnAxis(ap=idst[:, 0:1], axis=0)
                                      ).then_inc(ev("current").sem, 16)
                ev("new_rows").wait(gp, c + 1)
                ev("put_index").wait_alone(gp, c + 1, ev("pool_tally"))
                gp.indirect_dma_start(agg_d, bass.IndirectOffsetOnAxis(ap=iput[:, 0:1], axis=0), newr[:, :], None,
                                      bounds_check=N - 1, oob_is_err=False).then_inc(ev("st_rows").sem, 16)
                ev("st_rows").wait(gp, c * 16 + 16)
                gp.sem_inc(ev("scattered").sem, 1)
            gp.sem_inc(ev("edges_done").sem, 1)

        @block.gpsimd
        def _(gp):
            gp.memset(ident[:, :], 1.0).then_inc(ev("pool_set").sem, 1)
            gp.memset(ones[:, :], 1.0).then_inc(ev("ones").sem, 1)
            gp.memset(eb2x[:, :], 0.0).then_inc(ev("zeroed").sem, 1)
            gp.memset(pad_w[:, :], (1 << 30) - 1).then_inc(ev("pad").sem, 1)
            gp.iota(thr_i[:, :], pattern=[[P * G, TG]], base=0, channel_multiplier=G).then_inc(ev("thr_i").sem, 1)
            gp.iota(base_i[:, :], pattern=[[P * GW, TG]], base=0, channel_multiplier=GW).then_inc(ev("thr_i").sem, 1)
            gp.iota(iota_i[:, :], pattern=[[1, GW]], base=0, channel_multiplier=0).then_inc(ev("iota_i").sem, 1)
            ev("pool_set").wait(gp, 1)
            gp.affine_select(out=ident[:, :], in_=ident[:, :], compare_op=ALU.is_equal, fill=0.0, base=0,
                             pattern=[[-1, 128]], channel_multiplier=1).then_inc(ev("ident").sem, 1)
            for b in range(TG):
                ev("block").wait(gp, 1)
                gp.indirect_dma_start(blk[:, b, :], None, dst.rearrange("(c b) -> c b", b=BL),
                                      bass.IndirectOffsetOnAxis(ap=idx_b[:, b:b + 1], axis=0)).then_inc(ev("ld_blocks").sem, 16)
            ev("starts").wait(gp, 1)
            ev("st_chunks").wait(gp, 16)
            for b in range(TG):
                for h in range(2):
                    gp.indirect_dma_start(chunks[:, b, h, :], None, chunk_d,
                                          bass.IndirectOffsetOnAxis(ap=idx_c[:, h, b:b + 1], axis=0)).then_inc(ev("ld_chunks%d" % (b // TH)).sem, 16)

            with quick(gp):
                gp.tensor_copy(ident16[:, :], ident[0:P, 0:P]).then_inc(ev("ident16").sem, 1)
                with gp.Fori(0, S) as i:
                    for n, part in enumerate((xhi, xlo)):
                        ev("h_T").wait_alone(gp, i, ev("pool_tally"))
                        gp.tensor_copy(xst[:, n, :, :], part[:, bass.ds(i * A, A), :]).then_inc(ev("self_rows").sem, 1)
            with gp.Else():
                gp.memset(before_g[:, :], 1.0).then_inc(ev("pool_set").sem, 1)
                gp.memset(ones_g[:, :], 1.0).then_inc(ev("ones_g").sem, 1)
                ev("pool_set").wait(gp, 2)
                gp.affine_select(out=before_g[:, :], in_=before_g[:, :], compare_op=ALU.is_gt, fill=0.0, base=0,
                                 pattern=[[-1, P]], channel_multiplier=1).then_inc(ev("before").sem, 1)
                ev("xn_stored").wait(gp, NT)
                sum_over_edges(gp)
            with gp.Fori(0, S) as i:
                for k in range(KH):
                    ev("relu").wait_alone(gp, i * KH + k + 1, ev("pool_tally"))
                    ev("mm_w2").wait_alone(gp, i * KH - KH + k + 1, ev("pool_tally"))
                    gp.tensor_copy(rhi[:, k, :], rf[:, k, :]).then_inc(ev("r_hi").sem, 1)
            ev("ld_e1").wait(gp, 16)
            gp.tensor_copy(e1hi[:, :, :, :], estage[:, :, :, :]).then_inc(ev("e1_hi").sem, 1)
            ev("e1_hi").wait(gp, 1)
            gp.tensor_tensor(e1lo[:, :, :, :], estage[:, :, :, :], e1hi[:, :, :, :].bitcast(F32), ALU.subtract).then_inc(ev("e1_split").sem, 2)
            ev("ld_e2").wait(gp, 16)
            for e in range(NX):
                gp.tensor_copy(e2hi[:, e, :, :], estage[:, e, :, :]).then_inc(ev("e2_hi").sem, 1)
                ev("e2_hi").wait(gp, e + 1)
                gp.tensor_tensor(e2lo[:, e, :, :], estage[:, e, :, :], e2hi[:, e, :, :].bitcast(F32), ALU.subtract).then_inc(ev("e2_split").sem, 1)

        @block.scalar
        def _(ac):
            ev("var").wait(ac, 1)
            ac.activation(rs[:, 1, :], rs[:, 0, :], ACT.Sqrt).then_inc(ev("sd").sem, 1)

            def copy_h1(i, j):
                ev("mm_w1").wait(ac, i * KH + 2 * j + 2)
                if j == 0:
                    ev("h1st_free").wait(ac, i - 1)
                    ev("h1_stat").wait(ac, (i - 1) * KH)
                ac.copy(h1st[:, bass.ds(i % 2, 1), j * 512:(j + 1) * 512].rearrange("p a (m n) -> p (a m) n", m=2)[:, :, 0:C],
                        ps[:, 5 + j % 3, :].rearrange("p (m n) -> p m n", m=2)[:, :, 0:C]).then_inc(ev("h1_copied").sem, 1)
            for g in range(XG):
                ev("x_norm").wait(ac, (g + 1) * XT)
                ac.copy(xhi[:, g * XT:(g + 1) * XT, :], xs[:, g * XT:(g + 1) * XT, :]).then_inc(ev("x_hi").sem, 1)

            def counts(s, j):
                ev("counted").wait(ac, s * JB + j + 1)
                ac.copy(adj[:, bass.ds(s % 2, 1), :, j * 2 * G:(j + 1) * 2 * G].rearrange("p a t d -> p (a t) d"),
                        ps[0:P, j % 3, 0:2 * GW].rearrange("p (d t) -> p t d", t=NT)).then_inc(ev("adj").sem, 1)

            def quick_step(i, first=False, last=False):
                for what, n in order(first, last):
                    if what == "B":
                        counts(i + 1, n)
                    if what == "F" and n % 2:
                        copy_h1(i - 1, n // 2)

            with quick(ac):
                for j in range(JB):
                    counts(0, j)
                quick_step(0, first=True)
                with ac.Fori(1, S - 1) as i:
                    quick_step(i)
                quick_step(S - 1, last=True)
                for j in range(KH // 2):
                    copy_h1(S - 1, j)
            with ac.Else():
                with ac.Fori(0, S) as i:
                    for j in range(KH // 2):
                        copy_h1(i, j)
            ev("bn_var").wait(ac, 1)
            ac.activation(bns[:, 1, :], bns[:, 0, :], ACT.Sqrt).then_inc(ev("bn_sd").sem, 1)
            ev("bn_done").wait(ac, 1)
            def relu(i):
                ev("hin_ready").wait(ac, i + 1)
                for k in range(KH):
                    ev("r_lo").wait(ac, i * KH - KH + k + 1)
                    op = ac.activation(rf[:, k, :], hin[:, bass.ds(i % 2, 1), k * C:(k + 1) * C].rearrange("p a n -> p (a n)"),
                                       ACT.Relu, bias=bns[:, 5, k:k + 1], scale=bns[:, 4, k:k + 1])
                    op.then_inc(ev("relu").sem, 1)
            def sqrt_tok(i):
                ev("var_x").wait(ac, i + 1)
                ac.activation(rsb[:, 1, :], rsb[:, 0, :], ACT.Sqrt).then_inc(ev("sd_x").sem, 1)
            def copy_tT(i):
                ev("tok_T").wait(ac, i + 1)
                ev("router").wait(ac, i)
                ev("tT_stored").wait(ac, i)
                ac.copy(tTs[:, :, :], ps[:, 4, :].rearrange("p (k n) -> p k n", n=256)[:, :, 0:C]).then_inc(ev("tTs").sem, 1)
                ev("tTs").wait(ac, i + 1)
                ac.dma_start(tT_d[bass.ds(i, 1), :, :].rearrange("a p n -> p (a n)"), tTs[:, :, :].rearrange("p k n -> p (k n)")
                             ).then_inc(ev("st_tT").sem, 16)
            def stored_tT(i):
                ev("st_tT").wait(ac, i * 16 + 16)
                ac.sem_inc(ev("tT_stored").sem, 1)
            def relu_done(i):
                ev("relu").wait(ac, (i + 1) * KH)
                ac.sem_inc(ev("relu_step").sem, 1)
            relu(0)
            relu_done(0)
            relu(1)
            sqrt_tok(0)
            relu_done(1)
            with ac.Fori(2, S) as i:
                relu(i)
                copy_tT(i - 2)
                sqrt_tok(i - 1)
                stored_tT(i - 2)
                relu_done(i)
            copy_tT(S - 2)
            sqrt_tok(S - 1)
            stored_tT(S - 2)
            copy_tT(S - 1)
            stored_tT(S - 1)
            ev("gmax").wait(ac, 1)
            ac.activation(gt[:, :, :], gk[:, :, :], ACT.Exp).then_inc(ev("gexp").sem, 1)
            ev("ld_eb1").wait(ac, KD * 16)
            with ac.Fori(0, S) as i:
                for e in range(NX):
                    if e == 1:
                        ev("comb_T").wait(ac, i + 1)
                        ev("b2mm").wait(ac, i)
                        ac.copy(cT[:, :], ps[0:A * NX, 4, 0:P]).then_inc(ev("cT").sem, 1)
                    for j in range(KD):
                        ev("mm1").wait(ac, (i * NX + e) * KD + KD)
                        ev("g_split").wait(ac, 2 * (i * NX + e - 1))
                        ac.activation(gf[:, e % 2, j, :], ps[:, e % 2, j * 256:j * 256 + C], ACT.Gelu,
                                      bias=eb1T[:, e, j:j + 1]).then_inc(ev("gelu").sem, 1)

        @block.vector
        def _(dv):
            def rsqrt(r, width, sd_event, count, name, i=0, var=0):
                e = ev(name)
                base = i * 5
                sd_event.wait(dv, count)
                dv.reciprocal(r[:, 2, :], r[:, 1, :]).then_inc(e.sem, 1)
                e.wait(dv, base + 1)
                dv.tensor_tensor(r[:, 3, :], r[:, 2, :], r[:, 2, :], ALU.mult).then_inc(e.sem, 1)
                e.wait(dv, base + 2)
                dv.tensor_tensor(r[:, 3, :], r[:, 3, :], r[:, 0, :], ALU.mult).then_inc(e.sem, 1)
                e.wait(dv, base + 3)
                dv.tensor_scalar(r[:, 3, :], r[:, 3, :], -0.5, 1.5, ALU.mult, ALU.add).then_inc(e.sem, 1)
                e.wait(dv, base + 4)
                dv.tensor_tensor(r[:, 4, :], r[:, 2, :], r[:, 3, :], ALU.mult).then_inc(e.sem, 1)
                e.wait(dv, base + 5)

            ev("rw_T").wait(dv, 1)
            dv.tensor_copy(rwT[:, :, :], ps[:, 2, 0:KD * NX].rearrange("p (k e) -> p k e", k=KD)).then_inc(ev("rwT").sem, 1)
            n = [0]

            def step(ins):
                n[0] += 1
                ins.then_inc(ev("prep").sem, 1)
                ev("prep").wait(dv, n[0])

            ev("ld_src").wait(dv, 16)
            step(dv.tensor_scalar(sh_i[:, :], src_i[:, :], 1.0 / P, -0.5 * (P - 1) / P, ALU.mult, ALU.add))
            dv.scalar_tensor_tensor(out=src_i[:, :], in0=sh_i[:, :], scalar=-float(P), in1=src_i[:, :], op0=ALU.mult, op1=ALU.add).then_inc(ev("src_row").sem, 1)
            ev("ld_dst").wait(dv, 16)
            step(dv.scalar_tensor_tensor(out=sh_i[:, :], in0=dst_i[:, :], scalar=float(NT), in1=sh_i[:, :], op0=ALU.mult, op1=ALU.add))
            ev("src_row").wait(dv, 1)
            step(dv.tensor_scalar(sh_i[:, :], sh_i[:, :], 7, None, ALU.logical_shift_left))
            dv.tensor_tensor(word_i[:, :], sh_i[:, :], src_i[:, :], ALU.bitwise_or).then_inc(ev("words").sem, 1)
            ev("thr_i").wait(dv, 2)
            dv.tensor_copy(thr[:, :], thr_i[:, :]).then_inc(ev("thr").sem, 1)
            dv.tensor_copy(base_g[:, :], base_i[:, :]).then_inc(ev("thr").sem, 1)
            ev("ld_first").wait(dv, 16)
            dv.tensor_copy(fblk[:, :], idx_first[:, :]).then_inc(ev("fblk").sem, 1)
            ev("iota_i").wait(dv, 1)
            dv.tensor_copy(iota16[:, :], iota_i[:, :]).then_inc(ev("iota16").sem, 1)
            ev("firsts").wait(dv, 2)
            ev("thr").wait(dv, 2)
            junk = sh_i[:, 0:NB].bitcast(F32)
            ev("words").wait(dv, 1)
            for b in range(TG):
                dv.tensor_scalar(junk.rearrange("p (a n) -> p a n", a=1), ps[0:P, 0:2, :].rearrange("p a n -> p (a n)")[:, 0:NB].rearrange("p (a n) -> p a n", a=1), thr[:, b:b + 1], None, ALU.is_lt, ALU.add,
                                 accum_out=starts[:, 0, b:b + 1]).then_inc(ev("coarse").sem, 1)
                ev("coarse").wait(dv, b + 1)
            step(dv.tensor_scalar(starts[:, 1, :], starts[:, 0, :], -1.0, 0.0, ALU.add, ALU.max))
            dv.tensor_copy(idx_b[:, :], starts[:, 1, :]).then_inc(ev("block").sem, 1)

            ev("ld_x").wait(dv, 16)
            with dv.Fori(0, NT) as t:
                dv.bn_stats(st6[:, bass.ds(t, 1), :].rearrange("p a n -> p (a n)"), xs[:, bass.ds(t, 1), :].rearrange("p a n -> p (a n)")).then_inc(ev("stats").sem, 1)
            ev("stats").wait(dv, NT)
            step(dv.tensor_tensor(mv[:, :, 0], st6[:, :, 1], st6[:, :, 4], ALU.add))
            step(dv.tensor_tensor(mv[:, :, 1], st6[:, :, 1], st6[:, :, 4], ALU.subtract))
            step(dv.tensor_tensor(rs[:, 1, :], st6[:, :, 2], st6[:, :, 5], ALU.add))
            step(dv.tensor_scalar(mv[:, :, 0], mv[:, :, 0], 0.5, None, ALU.mult))
            step(dv.tensor_tensor(mv[:, :, 1], mv[:, :, 1], mv[:, :, 1], ALU.mult))
            step(dv.tensor_scalar(rs[:, 1, :], rs[:, 1, :], 1.0 / D, LN_EPS, ALU.mult, ALU.add))
            dv.scalar_tensor_tensor(out=rs[:, 0, :], in0=mv[:, :, 1], scalar=0.25, in1=rs[:, 1, :], op0=ALU.mult, op1=ALU.add).then_inc(ev("var").sem, 1)
            ev("var").wait(dv, 1)
            rsqrt(rs, NT, ev("sd"), 1, "rsq_x")
            step(dv.tensor_scalar(rs[:, 4, :], rs[:, 4, :], X_SCALE, None, ALU.mult))
            with dv.Fori(0, NT) as t:
                xt = xs[:, bass.ds(t, 1), :].rearrange("p a n -> p (a n)")
                dv.tensor_scalar(xt, xt, mv[:, bass.ds(t, 1), 0:1].rearrange("p a n -> p (a n)"), rs[:, 4, bass.ds(t, 1)],
                                 ALU.subtract, ALU.mult).then_inc(ev("x_norm").sem, 1)

            ev("ld_blocks").wait(dv, TG * 16)
            for b in range(TG):
                dv.tensor_scalar(sh_i[:, 0:BL].bitcast(F32), blk[:, b, :], thr[:, b:b + 1], None, ALU.is_lt, ALU.add,
                                 accum_out=starts[:, 2, b:b + 1]).then_inc(ev("fine").sem, 1)
                ev("fine").wait(dv, b + 1)
            step(dv.scalar_tensor_tensor(out=idx_c[:, 0, :], in0=starts[:, 1, :], scalar=float(BL), in1=starts[:, 2, :], op0=ALU.mult, op1=ALU.add))
            step(dv.tensor_scalar(idx_c[:, 0, :], idx_c[:, 0, :], 5, None, ALU.logical_shift_right))
            dv.tensor_scalar(idx_c[:, 1, :], idx_c[:, 0, :], float(CH // Q), None, ALU.add).then_inc(ev("starts").sem, 1)

            for g in range(XG):
                ev("x_hi").wait(dv, g + 1)
                dv.tensor_tensor(xlo[:, g * XT:(g + 1) * XT, :], xs[:, g * XT:(g + 1) * XT, :], xhi[:, g * XT:(g + 1) * XT, :], ALU.subtract).then_inc(ev("x_lo").sem, 1)

            for half in range(2):
                tiles = range(half * TH, (half + 1) * TH)
                ev("ld_chunks%d" % half).wait(dv, TH * 32)
                words = chunks[:, half * TH:(half + 1) * TH, :, :].rearrange("p b h n -> p b (h n)")
                if half:
                    ev("chunk_T").wait(dv, TH)
                    ev("hits").wait(dv, 1)
                step(dv.tensor_scalar(c_tmp[:, :, :], words, 7, None, ALU.logical_shift_right))
                step(dv.tensor_tensor(c_key[:, :, :], c_tmp[:, :, :], base_g[:, half * TH:(half + 1) * TH].rearrange("p (b a) -> p b a", a=1).broadcast_to([P, TH, 2 * CH]), ALU.subtract))
                step(dv.tensor_scalar(c_tmp[:, :, :], words, 127, None, ALU.bitwise_and))
                dv.tensor_copy(c_sl[:, :, :], c_tmp[:, :, :]).then_inc(ev("keys").sem, 1)
                ev("keys").wait(dv, half + 1)
                step(dv.tensor_scalar(c_tmp[:, :, :].bitcast(F32), c_key[:, :, :], 0.0, None, ALU.is_ge))
                flat = lambda v: v.rearrange("p b n -> p (b n)")
                step(dv.scalar_tensor_tensor(out=flat(c_tmp[:, :, :]).bitcast(F32), in0=flat(c_key[:, :, :]), scalar=float(GW), in1=flat(c_tmp[:, :, :]).bitcast(F32),
                                             op0=ALU.is_lt, op1=ALU.mult))
                dv.tensor_reduce(hits[:, half:half + 1], flat(c_tmp[:, :, :]).bitcast(F32), AX.X, ALU.add).then_inc(ev("hits").sem, 1)
                for b in tiles:
                    ev("chunk_T").wait(dv, b + 1)
                    bank = ps[:, b % TH, 0:4 * P].rearrange("p (s h g) -> p s h g", s=2, h=2)
                    cols = lambda v: v[:, b * P * 2:(b + 1) * P * 2].rearrange("p (g h) -> p h g", h=2)
                    dv.tensor_scalar(cols(keyT), bank[:, 0, :, :], 1000.0, -1000.0, ALU.min, ALU.max).then_inc(ev("key_T").sem, 1)
                    dv.tensor_copy(cols(slT), bank[:, 1, :, :]).then_inc(ev("key_T").sem, 1)
            ev("total").wait(dv, 1)
            step(dv.tensor_scalar(flag_f[:, :], ps[0:1, 7, 0:1], float(E), None, ALU.is_equal))
            dv.tensor_copy(flag[:, :], flag_f[:, :]).then_inc(ev("flag").sem, 1)
            for nw, (lane, hi, lo, k) in enumerate((("ld_w1", w1hi, w1lo, KD), ("ld_w2", w2hi, w2lo, KH))):
                s3 = stage.rearrange("p (k h) -> p k h", k=k)
                ev(lane).wait(dv, 16)
                dv.tensor_copy(hi[:, :, :], s3).then_inc(ev("w_split").sem, 1)
                ev("w_split").wait(dv, 2 * nw + 1)
                dv.tensor_tensor(lo[:, :, :], s3, hi[:, :, :].bitcast(F32), ALU.subtract).then_inc(ev("w_split").sem, 1)

            def sum_over_edges_dve():
                with dv.Fori(0, NT) as t:
                    ev("xn_stored").wait(dv, t)
                    dv.tensor_scalar(newr[:, :], xs[:, bass.ds(t, 1), :].rearrange("p a n -> p (a n)"), 1.0 / X_SCALE, None, ALU.mult).then_inc(ev("xn_row").sem, 1)
                ev("xn_stored").wait(dv, NT)
                ev("ld_src").wait(dv, 32)
                ev("ld_dst").wait(dv, 32)
                ev("before").wait(dv, 1)
                ev("ident").wait(dv, 1)
                with dv.Fori(0, EC) as c:
                    ev("scattered").wait(dv, c)
                    dv.tensor_copy(isrc[:, :], src_t[:, bass.ds(c, 1)]).then_inc(ev("index").sem, 1)
                    dv.tensor_copy(idst[:, :], dst_t[:, bass.ds(c, 1)]).then_inc(ev("index").sem, 1)
                    dv.tensor_copy(fdst[:, :], dst_t[:, bass.ds(c, 1)]).then_inc(ev("fdst").sem, 1)
                    ev("fdst").wait(dv, c + 1)
                    dv.tensor_scalar(diag[:, :], ident[0:P, 0:P], fdst[:, 0:1], None, ALU.mult).then_inc(ev("diag").sem, 1)
                    ev("dst_row").wait(dv, c + 1)
                    dv.tensor_scalar(sel[:, :], ps[0:P, 0, 0:P], fdst[:, 0:1], None, ALU.is_equal).then_inc(ev("sel").sem, 1)
                    ev("sel").wait(dv, c + 1)
                    dv.tensor_tensor_reduce(selb[:, :], sel[:, :], before_g[:, :], 1.0, 0.0, ALU.mult, ALU.add, rank[:, :]).then_inc(ev("rank").sem, 1)
                    ev("rank").wait(dv, c + 1)
                    dv.scalar_tensor_tensor(out=fput[:, :], in0=rank[:, :], scalar=float(N), in1=fdst[:, :], op0=ALU.mult, op1=ALU.add).then_inc(ev("fput").sem, 1)
                    ev("fput").wait(dv, c + 1)
                    dv.tensor_copy(iput[:, :], fput[:, :]).then_inc(ev("put_index").sem, 1)
                    ev("sel_mm").wait(dv, c + 1)
                    ev("current").wait(dv, c * 16 + 16)
                    dv.tensor_tensor(newr[:, :], ps[0:P, 1, 0:D], cur[:, :], ALU.add).then_inc(ev("new_rows").sem, 1)

            def split_h(i, scaled=False):
                ev("h_T").wait(dv, i + 1)
                ev("mm_w1").wait(dv, (i - 1) * KH)
                if scaled:
                    hT = ps[:, 3:3 + KD, 0:C]
                    scale = 1.0 / X_SCALE
                else:
                    hT = ps[:, 4, :].rearrange("p (k n) -> p k n", n=256)[:, :, 0:C]
                    scale = 1.0
                hi = hhi[:, bass.ds(i % 2, 1), :, :].rearrange("p a k n -> p (a k) n")
                lo = hlo[:, bass.ds(i % 2, 1), :, :].rearrange("p a k n -> p (a k) n")
                dv.tensor_scalar(hi, hT, scale, None, ALU.mult).then_inc(ev("h_hi").sem, 1)
                ev("h_hi").wait(dv, i + 1)
                dv.scalar_tensor_tensor(out=lo, in0=hT, scalar=scale, in1=hi.bitcast(F32), op0=ALU.mult, op1=ALU.subtract).then_inc(ev("h_split").sem, 1)

            def stats(i, m):
                if m % 2 == 0:
                    ev("h1_copied").wait_alone(dv, i * (KH // 2) + m // 2 + 1, ev("dve_tally"))
                dv.bn_stats(hstat[:, m, bass.ds(i, 1), :].rearrange("p a n -> p (a n)"),
                            h1st[:, bass.ds(i % 2, 1), m * 256:m * 256 + C].rearrange("p a n -> p (a n)")).then_inc(ev("h1_stat").sem, 1)

            def columns(s):
                at = bass.ds(s * 2 * SG, 2 * SG)
                ev("oh").wait(dv, s * JB)
                dv.tensor_copy(steps_k[:, 0, :], keyT[:, at]).then_inc(ev("columns").sem, 1)
                dv.tensor_copy(steps_k[:, 1, :], slT[:, at]).then_inc(ev("columns").sem, 1)
                ev("columns").wait(dv, s * 2 + 2)

            def one_hots(s, j):
                ev("counted").wait(dv, s * JB + j + 1 - RING)
                for c in range(4):
                    col = 4 * j + c
                    dv.tensor_scalar(oh_s[:, j % RING, c, :], iota16[:, 0:CH], steps_k[:, 1, col:col + 1], None, ALU.is_equal)
                    o = dv.tensor_scalar(oh_k[:, j % RING, c, :], iota16[:, :], steps_k[:, 0, col:col + 1], None, ALU.is_equal)
                o.then_inc(ev("oh").sem, 1)

            def quick_step(i, first=False, last=False):
                if not last:
                    columns(i + 1)
                todo = [n // 2 for what, n in order(first, last) if what == "F" and n % 2]
                after = {}
                b = 0
                for what, n in order(False, False):
                    b += what == "B"
                    if what == "F" and n % 2:
                        after[n // 2] = min(b + RING, JB - 1)
                for j in range(JB):
                    if not last:
                        one_hots(i + 1, j)
                    if j == RING - 1 and not first:
                        split_h(i - 1, True)
                    for p in todo:
                        if after[p] == j:
                            stats(i - 1, 2 * p)
                            stats(i - 1, 2 * p + 1)

            with quick(dv):
                columns(0)
                for j in range(JB):
                    one_hots(0, j)
                quick_step(0, first=True)
                with dv.Fori(1, S - 1) as i:
                    quick_step(i)
                quick_step(S - 1, last=True)
                split_h(S - 1, True)
                for m in range(KH):
                    stats(S - 1, m)
            with dv.Else():
                sum_over_edges_dve()
                split_h(0)
                with dv.Fori(0, S - 1) as i:
                    for m in range(KH):
                        stats(i, m)
                        if m == KH // 2:
                            split_h(i + 1)
                for m in range(KH):
                    stats(S - 1, m)
            ev("h1_stat").wait(dv, S * KH)
            for m in range(KH):
                dv.bn_aggr(hmv[:, m, :], hstat[:, m, :, :].rearrange("p a n -> p (a n)")).then_inc(ev("hmv").sem, 1)
            ev("hmv").wait(dv, KH)
            ev("ld_bn").wait(dv, 48)
            dv.tensor_scalar(bns[:, 0, :], hmv[:, :, 1], BN_EPS, None, ALU.add).then_inc(ev("bn_var").sem, 1)
            dv.tensor_tensor(bns[:, 6, :], hmv[:, :, 0], bnp[:, 0, :], ALU.add).then_inc(ev("bn_mean").sem, 1)
            rsqrt(bns, KH, ev("bn_sd"), 1, "rsq_h")
            dv.tensor_tensor(bns[:, 7, :], bns[:, 4, :], bnp[:, 1, :], ALU.mult).then_inc(ev("bn_s").sem, 1)
            ev("bn_mean").wait(dv, 1)
            dv.tensor_tensor(bns[:, 6, :], bnp[:, 0, :], bns[:, 6, :], ALU.subtract).then_inc(ev("bn_s").sem, 1)
            ev("bn_s").wait(dv, 2)
            dv.tensor_tensor(bns[:, 6, :], bns[:, 6, :], bns[:, 7, :], ALU.mult).then_inc(ev("bn_s").sem, 1)
            dv.tensor_copy(bns[:, 4, :], bns[:, 7, :]).then_inc(ev("bn_s").sem, 1)
            ev("bn_s").wait(dv, 4)
            dv.tensor_tensor(bns[:, 5, :], bns[:, 6, :], bnp[:, 2, :], ALU.add).then_inc(ev("bn_t").sem, 1)
            ev("bn_t").wait(dv, 1)
            dv.sem_inc(ev("bn_done").sem, 1)

            def lower(i):
                for k in range(KH):
                    ev("r_hi").wait(dv, i * KH + k + 1)
                    ev("mm_w2").wait(dv, i * KH - KH + k + 1)
                    dv.tensor_tensor(rlo[:, k, :], rf[:, k, :], rhi[:, k, :].bitcast(F32), ALU.subtract).then_inc(ev("r_lo").sem, 1)

            def rows(i):
                xi = xs[:, bass.ds(i * A, A), :]
                ev("mm_w2").wait(dv, (i + 1) * KH)
                for a in range(A):
                    dv.tensor_tensor(vt[:, a, :], ps[0:P, bass.ds((i % 2) * A + a, 1), 0:D].rearrange("p a n -> p (a n)"), b2bc[:, 0, :], ALU.add).then_inc(ev("psO_read").sem, 1)
                ev("psO_read").wait(dv, i * A + A)
                dv.scalar_tensor_tensor(out=xi, in0=vt[:, :, :], scalar=0.0, in1=xi, op0=ALU.max, op1=ALU.add).then_inc(ev("x2").sem, 1)
                ev("x2").wait_alone(dv, i + 1, ev("dve_tally"))
                for a in range(A):
                    dv.bn_stats(s6b[:, a, :], xs[:, bass.ds(i * A + a, 1), :].rearrange("p a n -> p (a n)")).then_inc(ev("stats_x").sem, 1)
                ev("stats_x").wait_alone(dv, i * A + A, ev("dve_tally"))
                for a in range(A):
                    dv.bn_aggr(mvb[:, a, :], s6b[:, a, :]).then_inc(ev("mv_x").sem, 1)
                ev("mv_x").wait(dv, i * A + A)
                dv.tensor_scalar(rsb[:, 0, :], mvb[:, :, 1], LN_EPS, None, ALU.add).then_inc(ev("var_x").sem, 1)
                rsqrt(rsb, A, ev("sd_x"), i + 1, "rsq_t", i)
                ev("tok_T").wait(dv, i)
                for a in range(A):
                    dv.tensor_scalar(tok[:, a, :], xs[:, bass.ds(i * A + a, 1), :].rearrange("p a n -> p (a n)"),
                                     mvb[:, a, 0:1], rsb[:, 4, a:a + 1], ALU.subtract, ALU.mult).then_inc(ev("tok").sem, 1)
                ev("tok").wait(dv, i * A + A)
                dv.tensor_tensor(xi, xi, tok[:, :, :], ALU.add).then_inc(ev("x3").sem, 1)

            def logits(i):
                ev("router").wait(dv, i + 1)
                dv.tensor_copy(L[:, bass.ds(i * A, A), :], ps[0:P, 5, 0:A * NX].rearrange("p (a e) -> p a e", a=A)).then_inc(ev("logits").sem, 1)

            ev("ld_b2").wait(dv, 16)
            ev("ld_x").wait(dv, 32)
            lower(0)
            lower(1)
            rows(0)
            with dv.Fori(2, S) as i:
                lower(i)
                rows(i - 1)
                logits(i - 2)
            logits(S - 2)
            rows(S - 1)
            logits(S - 1)

            n[0] = 0

            def step(ins):
                n[0] += 1
                ins.then_inc(ev("gate").sem, 1)
                ev("gate").wait(dv, n[0])
            wide = lambda v: v.rearrange("p (t a) -> p t a", a=1).broadcast_to([P, NT, NX])
            ev("logits").wait(dv, S)
            step(dv.tensor_reduce(gm[:, 0, :], L[:, :, :], AX.X, ALU.max))
            dv.tensor_tensor(gk[:, :, :], L[:, :, :], wide(gm[:, 0, :]), ALU.subtract).then_inc(ev("gmax").sem, 1)
            ev("gexp").wait(dv, 1)
            step(dv.tensor_reduce(gm[:, 1, :], gt[:, :, :], AX.X, ALU.add))
            step(dv.reciprocal(gm[:, 1, :], gm[:, 1, :]))
            step(dv.tensor_tensor(L[:, :, :], gt[:, :, :], wide(gm[:, 1, :]), ALU.mult))
            step(dv.memset(gk[:, :, :], 0.0))
            for j in range(NX):
                pj = lambda a, b: L[:, :, j:j + 1].broadcast_to([P, NT, b - a])
                for a, b, op in ((0, j, ALU.is_gt), (j + 1, NX, ALU.is_ge)):
                    if a < b:
                        step(dv.tensor_tensor(gt[:, :, a:b], pj(a, b), L[:, :, a:b], op))
                        step(dv.tensor_tensor(gk[:, :, a:b], gk[:, :, a:b], gt[:, :, a:b], ALU.add))
            step(dv.tensor_scalar(gk[:, :, :], gk[:, :, :], 2.0, None, ALU.is_lt))
            step(dv.tensor_tensor(L[:, :, :], L[:, :, :], gk[:, :, :], ALU.mult))
            step(dv.tensor_reduce(gm[:, 2, :], L[:, :, :], AX.X, ALU.add))
            step(dv.tensor_scalar(gm[:, 2, :], gm[:, 2, :], 1e-12, None, ALU.max))
            step(dv.reciprocal(gm[:, 2, :], gm[:, 2, :]))
            step(dv.tensor_tensor(L[:, :, :], L[:, :, :], wide(gm[:, 2, :]), ALU.mult))
            dv.sem_inc(ev("gnn_done").sem, 1)

            def split_t(i):
                ev("tin_ready").wait(dv, i + 1)
                ev("mm1").wait(dv, (i - 1) * NX * KD)
                t = tin[:, bass.ds(i % 2, 1), :].rearrange("p a (k n) -> p (a k) n", k=KD)
                hi = thi[:, bass.ds(i % 2, 1), :, :].rearrange("p a k n -> p (a k) n")
                lo = tlo[:, bass.ds(i % 2, 1), :, :].rearrange("p a k n -> p (a k) n")
                dv.tensor_copy(hi, t).then_inc(ev("t_split").sem, 1)
                ev("t_split").wait(dv, i * 2 + 1)
                dv.tensor_tensor(lo, t, hi.bitcast(F32), ALU.subtract).then_inc(ev("t_split").sem, 1)

            def gates(i):
                ev("comb_T").wait(dv, i)
                dv.tensor_copy(cst[:, :], L[:, bass.ds(i * A, A), :].rearrange("p a e -> p (a e)")).then_inc(ev("cst").sem, 1)

            def split_g(i, e):
                n = i * NX + e
                ev("gelu").wait(dv, n * KD + KD)
                ev("mm2").wait(dv, n - 1)
                dv.tensor_copy(ghi[:, e % 2, :, :], gf[:, e % 2, :, :]).then_inc(ev("g_split").sem, 1)
                ev("g_split").wait(dv, 2 * n + 1)
                dv.tensor_tensor(glo[:, e % 2, :, :], gf[:, e % 2, :, :], ghi[:, e % 2, :, :].bitcast(F32), ALU.subtract).then_inc(ev("g_split").sem, 1)

            def add_y(i, e):
                n = i * NX + e
                ev("mm2").wait(dv, n + 1)
                ev("y_added").wait(dv, n * A)
                for a in range(A):
                    xa = xs[:, bass.ds(i * A + a, 1), :].rearrange("p a n -> p (a n)")
                    dv.scalar_tensor_tensor(out=xa, in0=ps[0:P, 2 + e % 2, a * D:(a + 1) * D], scalar=L[:, bass.ds(i * A + a, 1), e:e + 1].rearrange("p a n -> p (a n)"),
                                            in1=xa, op0=ALU.mult, op1=ALU.add).then_inc(ev("y_added").sem, 1)

            def add_b2(i):
                ev("b2mm").wait(dv, i + 1)
                ev("y_added").wait(dv, (i + 1) * NX * A)
                xi = xs[:, bass.ds(i * A, A), :]
                dv.tensor_tensor(xi, ps[0:P, 5, :].rearrange("p (a d) -> p a d", a=A), xi, ALU.add).then_inc(ev("acc").sem, 1)

            def experts(i, last):
                for e in range(NX):
                    split_g(i, e)
                    if e:
                        add_y(i, e - 1)
                    if e == NX // 2 and not last:
                        split_t(i + 1)
                        gates(i + 1)
                add_y(i, NX - 1)
                add_b2(i)

            ev("x3").wait(dv, S)
            split_t(0)
            gates(0)
            with dv.Fori(0, S - 1) as i:
                experts(i, False)
            experts(S - 1, True)

        @block.tensor
        def _(pe):
            def mm3(o, left, right, start, stop):
                (lh, ll), (rh, rl) = left, right
                pe.matmul(o, lh, rh, start=start, stop=False)
                pe.matmul(o, lh, rl, start=False, stop=False)
                return pe.matmul(o, ll, rh, start=False, stop=stop)

            ev("ident").wait(pe, 1)
            ev("ld_rw").wait(pe, 16)
            for k in range(KD):
                t = pe.transpose(ps[:, 2, k * NX:(k + 1) * NX], rw_rows[:, k * 128:(k + 1) * 128], ident[0:NX, 0:NX])
            t.then_inc(ev("rw_T").sem, 1)

            ev("ones").wait(pe, 1)
            ev("fblk").wait(pe, 1)
            for half, at in enumerate((slice(0, 512), slice(512, NB))):
                pe.matmul(ps[0:P, half, 0:at.stop - at.start], ones[0:1, :], fblk[0:1, at], start=True, stop=True).then_inc(ev("firsts").sem, 1)
            ev("coarse").wait(pe, TG)
            for half in range(2):
                ev("keys").wait(pe, half + 1)
                for b in range(half * TH, (half + 1) * TH):
                    if half:
                        ev("key_T").wait(pe, 2 * (b - TH) + 2)
                    for n, v in enumerate((c_key, c_sl)):
                        for h in range(2):
                            at = (2 * n + h) * P
                            t = pe.transpose(ps[:, b % TH, at:at + P], v[:, b - half * TH, h * CH:(h + 1) * CH], ident[0:P, 0:P])
                    t.then_inc(ev("chunk_T").sem, 1)
            ev("hits").wait(pe, 2)
            for half in range(2):
                t = pe.matmul(ps[0:1, 7, 0:1], hits[:, half:half + 1], ones[:, 0:1], start=half == 0, stop=half == 1)
            t.then_inc(ev("total").sem, 1)

            def sum_over_edges_pe():
                ev("ones_g").wait(pe, 1)
                with pe.Fori(0, EC) as c:
                    ev("diag").wait(pe, c + 1)
                    pe.matmul(ps[0:P, 0, 0:P], ones_g[:, :], diag[:, :], start=True, stop=True).then_inc(ev("dst_row").sem, 1)
                    ev("sel").wait(pe, c + 1)
                    ev("gathered").wait(pe, c * 16 + 16)
                    pe.matmul(ps[0:P, 1, 0:D], sel[:, :], grow[:, :], start=True, stop=True).then_inc(ev("sel_mm").sem, 1)

            def transpose_h(i):
                ev("ld_h").wait(pe, i * 16 + 16)
                ev("h_split").wait(pe, i)
                for a in range(A):
                    for k in range(KD):
                        t = pe.transpose(ps[:, 4, k * 256 + a * P:k * 256 + (a + 1) * P], hb[:, a, k * 128:(k + 1) * 128], ident[0:P, 0:P])
                t.then_inc(ev("h_T").sem, 1)

            def first_block(i, m):
                if m == 0:
                    ev("h_split").wait(pe, i + 1)
                if m % 2 == 0:
                    j = m // 2
                    ev("h1_copied").wait(pe, i * (KH // 2) + (0, -2, -1, 1)[j])
                for k in range(KD):
                    w = [v[:, k, m * 128:(m + 1) * 128] for v in (w1hi, w1lo)]
                    h = [v[:, bass.ds(i % 2, 1), k, :].rearrange("p a n -> p (a n)") for v in (hhi, hlo)]
                    t = mm3(ps[:, 5 + m // 2 % 3, (m % 2) * 256:(m % 2) * 256 + C], w, h, k == 0, k == KD - 1)
                t.then_inc(ev("mm_w1").sem, 1)

            def first_product(i, last):
                for m in range(KH):
                    first_block(i, m)
                    if m == KH // 4 and not last:
                        transpose_h(i + 1)

            def count(s, j):
                ev("oh").wait(pe, s * JB + j + 1)
                ev("adj").wait(pe, s * JB + j + 1 - 3 + (2 if j == 0 else 0))
                for g in range(2):
                    for c in range(2):
                        t = pe.matmul(ps[0:P, j % 3, g * GW:(g + 1) * GW], oh_s[:, j % RING, 2 * g + c, 0:P], oh_k[:, j % RING, 2 * g + c, :],
                                      start=c == 0, stop=c == 1)
                t.then_inc(ev("counted").sem, 1)

            def gather_sum(i, j):
                if j == 0:
                    ev("adj").wait(pe, (i + 1) * JB)
                    ev("h_split").wait(pe, i)
                for t in (2 * j, 2 * j + 1):
                    a = adj[:, bass.ds(i % 2, 1), t, :].rearrange("p a n -> p (a n)")
                    for k in range(KD):
                        for n, part in enumerate((xhi, xlo)):
                            pe.matmul(ps[:, 3 + k, 0:C], part[:, t, k * 128:(k + 1) * 128], a, start=t == 0 and n == 0, stop=False)
                if j == JB - 1:
                    ev("self_rows").wait(pe, i * 2 + 2)
                    for k in range(KD):
                        for a in range(A):
                            for n in range(2):
                                m = pe.matmul(ps[:, 3 + k, a * P:(a + 1) * P], xst[:, n, a, k * 128:(k + 1) * 128], ident16[:, :],
                                              start=False, stop=n == 1 and a == 1)
                    m.then_inc(ev("h_T").sem, 1)

            def quick_step(i, first=False, last=False):
                for what, n in order(first, last):
                    if what == "B":
                        count(i + 1, n)
                    if what == "F":
                        first_block(i - 1, n)
                    if what == "G":
                        gather_sum(i, n)

            with quick(pe):
                ev("ident16").wait(pe, 1)
                ev("x_lo").wait(pe, XG)
                for j in range(JB):
                    count(0, j)
                ev("w_split").wait(pe, 4)
                quick_step(0, first=True)
                with pe.Fori(1, S - 1) as i:
                    quick_step(i)
                quick_step(S - 1, last=True)
                for m in range(KH):
                    first_block(S - 1, m)
            with pe.Else():
                sum_over_edges_pe()
                ev("w_split").wait(pe, 4)
                transpose_h(0)
                with pe.Fori(0, S - 1) as i:
                    first_product(i, False)
                first_product(S - 1, True)

            def second_product(i):
                ev("psO_read").wait(pe, (i - 1) * A)
                for k in range(KH):
                    ev("r_lo").wait(pe, i * KH + k + 1)
                    for a in range(A):
                        r = [v[:, k, a * P:(a + 1) * P] for v in (rhi, rlo)]
                        w = [v[:, k, :] for v in (w2hi, w2lo)]
                        t = mm3(ps[0:P, bass.ds((i % 2) * A + a, 1), 0:D].rearrange("p a n -> p (a n)"), r, w, k == 0, k == KH - 1)
                    t.then_inc(ev("mm_w2").sem, 1)

            def transpose_tok(i):
                ev("tok").wait(pe, i * A + A)
                ev("tTs").wait(pe, i)
                for a in range(A):
                    for k in range(KD):
                        t = pe.transpose(ps[:, 4, k * 256 + a * P:k * 256 + (a + 1) * P], tok[:, a, k * 128:(k + 1) * 128], ident[0:P, 0:P])
                t.then_inc(ev("tok_T").sem, 1)

            def router(i):
                ev("tTs").wait(pe, i + 1)
                ev("logits").wait(pe, i)
                for a in range(A):
                    for k in range(KD):
                        t = pe.matmul(ps[0:P, 5, a * NX:(a + 1) * NX], tTs[:, k, a * P:(a + 1) * P], rwT[:, k, :], start=k == 0, stop=k == KD - 1)
                t.then_inc(ev("router").sem, 1)

            ev("rwT").wait(pe, 1)
            second_product(0)
            second_product(1)
            transpose_tok(0)
            with pe.Fori(2, S) as i:
                second_product(i)
                router(i - 2)
                transpose_tok(i - 1)
            router(S - 2)
            transpose_tok(S - 1)
            router(S - 1)

            def layer1(i, e):
                ev("e1_split").wait(pe, 2)
                ev("gelu").wait(pe, (i * NX + e - 1) * KD)
                ev("t_split").wait(pe, i * 2 + 2)
                for j in range(KD):
                    for k in range(KD):
                        w = [v[:, e, k, j * 128:(j + 1) * 128] for v in (e1hi, e1lo)]
                        t = [v[:, bass.ds(i % 2, 1), k, :].rearrange("p a n -> p (a n)") for v in (thi, tlo)]
                        m = mm3(ps[:, e % 2, j * 256:j * 256 + C], w, t, k == 0, k == KD - 1)
                    m.then_inc(ev("mm1").sem, 1)

            def layer2(i, e):
                n = i * NX + e
                ev("e2_split").wait(pe, e + 1)
                ev("g_split").wait(pe, 2 * n + 2)
                ev("y_added").wait(pe, (n - 1) * A)
                for a in range(A):
                    for j in range(KD):
                        g = [v[:, e % 2, j, a * P:(a + 1) * P] for v in (ghi, glo)]
                        w = [v[:, e, j, :] for v in (e2hi, e2lo)]
                        m = mm3(ps[0:P, 2 + e % 2, a * D:(a + 1) * D], g, w, j == 0, j == KD - 1)
                m.then_inc(ev("mm2").sem, 1)

            def second_bias(i):
                ev("cst").wait(pe, i + 1)
                pe.transpose(ps[0:A * NX, 4, 0:P], cst[:, :], ident[0:P, 0:P]).then_inc(ev("comb_T").sem, 1)

            def second_bias_mm(i):
                ev("cT").wait(pe, i + 1)
                ev("acc").wait(pe, i)
                ev("ld_eb2").wait(pe, A * 16)
                pe.matmul(ps[0:P, 5, :], cT[:, :], eb2x[:, :], start=True, stop=True).then_inc(ev("b2mm").sem, 1)

            def pe_experts(i, last):
                for e in range(NX):
                    if e == 0:
                        second_bias(i)
                    if e + 1 < NX:
                        layer1(i, e + 1)
                    elif not last:
                        layer1(i + 1, 0)
                    if e == 4:
                        second_bias_mm(i)
                    layer2(i, e)

            ev("gnn_done").wait(pe, 1)
            layer1(0, 0)
            with pe.Fori(0, S - 1) as i:
                pe_experts(i, False)
            pe_experts(S - 1, True)


_INS = ["x", "src", "dst", "L0_gnn_W1", "L0_gnn_b1", "L0_gnn_gamma", "L0_gnn_beta", "L0_gnn_W2", "L0_gnn_b2",
        "L0_ffn_router_w", "L0_ffn_w1", "L0_ffn_b1", "L0_ffn_w2", "L0_ffn_b2"]


def kernel(**inputs):
    import numpy as _np
    import concourse.bacc as _bacc
    from concourse import mybir as _mybir
    from concourse.bass_utils import run_bass_kernel_spmd as _run

    nc = _bacc.Bacc("TRN2", target_bir_lowering=False, num_devices=1)
    arrays, args = {}, []
    for name in _INS:
        a = _np.ascontiguousarray(inputs[name])
        arrays[f"in_{name}_dram"] = a
        args.append(nc.dram_tensor(f"in_{name}_dram", a.shape, _mybir.dt.from_np(a.dtype), kind="ExternalInput").ap())
    out = nc.dram_tensor("out_dram", inputs["x"].shape, _mybir.dt.float32, kind="ExternalOutput").ap()
    gnn_moe(nc, *args, out)
    r = _run(nc, [arrays], core_ids=[0])
    return r.results[0]["out_dram"]
```
